# Optimizing a Trainium2 kernel written in Bass

```python
import numpy as np
import jax
import jax.numpy as jnp

def _softmax(x, axis=-1):
    return jax.nn.softmax(x, axis=axis)

def _gelu(x):
    return jax.nn.gelu(x, approximate=True)

def _silu(x):
    return jax.nn.silu(x)

def _sigmoid(x):
    return jax.nn.sigmoid(x)

def _layernorm(x, axis=-1, eps=1e-05):
    m = jnp.mean(x, axis=axis, keepdims=True)
    v = jnp.var(x, axis=axis, keepdims=True)
    return (x - m) / jnp.sqrt(v + eps)

def _scatter_add(tgt, idx, src, axis=0):
    return tgt.at[idx].add(src)

def _segment_sum(src, seg, n):
    return jax.ops.segment_sum(src, seg, n)
kernel_name = 'mk_cond_resid_d2_seqx_r4_062244'

def setup_inputs(seed: int=0):
    np.random.seed(seed)
    _w = jnp.asarray

    def _rec_inputs():
        import jax
        import jax.numpy as jnp
        _rk = jax.random.key(seed)
        x = -0.000125 + 0.9999 * jax.random.normal(jax.random.fold_in(_rk, 1), (8, 512, 256), jnp.float32)
        _lenS = 512 - jax.random.randint(jax.random.fold_in(_rk, 7), (8,), 0, max(1, 512 // 4) + 1, jnp.int32)
        _lenS2 = 512 - jax.random.randint(jax.random.fold_in(_rk, 8), (8,), 0, max(1, 512 // 4) + 1, jnp.int32)
        cond_1024 = -0.00493535 + 1.00056 * jax.random.normal(jax.random.fold_in(_rk, 11), (8, 256), jnp.float32)
        return (x, cond_1024)
    x, cond_1024 = _rec_inputs()

    def _L0_cond_setup():
        import jax, jax.numpy as jnp
        import numpy as np
        import math
        D = 256
        H = 256
        key = jax.random.key(seed)
        k1, k2, k3, k4 = jax.random.split(key, 4)
        x = jax.random.normal(k1, (64, 128, D), dtype=jnp.float32)
        h0 = jax.random.normal(k2, (64, H), dtype=jnp.float32)
        Wx = jax.random.normal(k3, (D, 4 * H), dtype=jnp.float32) / math.sqrt(D)
        Wh = jax.random.normal(k4, (H, 4 * H), dtype=jnp.float32) / math.sqrt(H)
        b = jnp.zeros((4 * H,), dtype=jnp.float32)
        return {'x': x, 'h0': h0, 'Wx': Wx, 'Wh': Wh, 'b': b}
    _L0_cond_all = _L0_cond_setup()
    _L0_cond_in = {k: v for k, v in _L0_cond_all.items() if k in ('Wx', 'Wh', 'b')}
    del _L0_cond_all

    def _L1_cond_setup():
        import jax, jax.numpy as jnp
        import numpy as np
        INPUT_DIM = 256
        LATENT_DIM = 256
        key = jax.random.key(seed)
        ks = jax.random.split(key, 8)
        B, T = (64, 128)
        concat_dim = INPUT_DIM + LATENT_DIM
        s = lambda fan_in: 1.0 / np.sqrt(fan_in)
        return {'x': jax.random.normal(ks[0], (B, T, INPUT_DIM), dtype=jnp.float32), 'h0': jax.random.normal(ks[1], (B, LATENT_DIM), dtype=jnp.float32), 'w_W': jax.random.uniform(ks[2], (concat_dim, 2 * LATENT_DIM), jnp.float32, -s(concat_dim), s(concat_dim)), 'w_b': jax.random.uniform(ks[3], (2 * LATENT_DIM,), jnp.float32, -s(concat_dim), s(concat_dim)), 'wx_W': jax.random.uniform(ks[4], (INPUT_DIM, LATENT_DIM), jnp.float32, -s(INPUT_DIM), s(INPUT_DIM)), 'wx_b': jax.random.uniform(ks[5], (LATENT_DIM,), jnp.float32, -s(INPUT_DIM), s(INPUT_DIM)), 'wh_W': jax.random.uniform(ks[6], (LATENT_DIM, LATENT_DIM), jnp.float32, -s(LATENT_DIM), s(LATENT_DIM)), 'wh_b': jax.random.uniform(ks[7], (LATENT_DIM,), jnp.float32, -s(LATENT_DIM), s(LATENT_DIM))}
    _L1_cond_all = _L1_cond_setup()
    _L1_cond_in = {k: v for k, v in _L1_cond_all.items() if k in ('w_W', 'w_b', 'wx_W', 'wx_b', 'wh_W', 'wh_b')}
    del _L1_cond_all
    return {'x': x, 'cond_1024': cond_1024, 'L0_cond_Wx': _L0_cond_in['Wx'], 'L0_cond_Wh': _L0_cond_in['Wh'], 'L0_cond_b': _L0_cond_in['b'], 'L1_cond_w_W': _L1_cond_in['w_W'], 'L1_cond_w_b': _L1_cond_in['w_b'], 'L1_cond_wx_W': _L1_cond_in['wx_W'], 'L1_cond_wx_b': _L1_cond_in['wx_b'], 'L1_cond_wh_W': _L1_cond_in['wh_W'], 'L1_cond_wh_b': _L1_cond_in['wh_b']}

def reference(x, cond_1024, L0_cond_Wx, L0_cond_Wh, L0_cond_b, L1_cond_w_W, L1_cond_w_b, L1_cond_wx_W, L1_cond_wx_b, L1_cond_wh_W, L1_cond_wh_b):
    import jax
    import jax.numpy as jnp

    def _L0_cond_ref(x, h0, Wx, Wh, b):
        import jax, jax.numpy as jnp
        import numpy as np
        import math
        D = 256
        H = 256
        Hdim = h0.shape[1]
        xW = jnp.einsum('ntd,dk->ntk', x, Wx) + b
        c0 = jnp.zeros_like(h0)

        def step(carry, xw_t):
            prev_h, prev_c = carry
            a = xw_t + prev_h @ Wh
            i = jax.nn.sigmoid(a[:, :Hdim])
            f = jax.nn.sigmoid(a[:, Hdim:2 * Hdim])
            o = jax.nn.sigmoid(a[:, 2 * Hdim:3 * Hdim])
            g = jnp.tanh(a[:, 3 * Hdim:])
            next_c = f * prev_c + i * g
            next_h = o * jnp.tanh(next_c)
            return ((next_h, next_c), next_h)
        xW_t = jnp.swapaxes(xW, 0, 1)
        _, hs = jax.lax.scan(step, (h0, c0), xW_t)
        hn = jnp.swapaxes(hs, 0, 1)
        return hn

    def _L1_cond_ref(x, h0, w_W, w_b, wx_W, wx_b, wh_W, wh_b):
        import jax, jax.numpy as jnp
        import numpy as np
        INPUT_DIM = 256
        LATENT_DIM = 256
        xT = jnp.swapaxes(x, 0, 1)

        def step(h, x_t):
            fused = jax.nn.sigmoid(jnp.concatenate([x_t, h], axis=-1) @ w_W + w_b)
            hidden_state, output_state = jnp.split(fused, 2, axis=-1)
            memory_state = x_t @ wx_W + wx_b + hidden_state * (h @ wh_W + wh_b)
            h_new = output_state * h + (1.0 - output_state) * jnp.tanh(memory_state)
            return (h_new, h_new)
        _, hs = jax.lax.scan(step, h0, xT)
        return jnp.swapaxes(hs, 0, 1)
    x = x + _L0_cond_ref(x, cond_1024, L0_cond_Wx, L0_cond_Wh, L0_cond_b)
    x = x + _L1_cond_ref(x, cond_1024, L1_cond_w_W, L1_cond_w_b, L1_cond_wx_W, L1_cond_wx_b, L1_cond_wh_W, L1_cond_wh_b)
    return x

_drawn_inputs = setup_inputs


def setup_inputs(seed=0):
    import zlib

    import numpy as np

    out = dict(_drawn_inputs(seed))
    spreads = {'L0_cond_b': (0.0, 0.1)}
    factors = {'L1_cond_w_b': 8.0, 'L1_cond_wh_b': 3.902}
    for name, (base, spread) in spreads.items():
        noise = np.random.default_rng([zlib.crc32(name.encode()), seed]).standard_normal(out[name].shape)
        drawn = base * np.exp(spread * noise) if base else spread * noise
        out[name] = jnp.asarray(drawn.astype(out[name].dtype))
    for name, factor in factors.items():
        out[name] = (out[name] * factor).astype(out[name].dtype)
    return out
```

```python
import concourse.bass as bass
from concourse import mybir
from contextlib import ExitStack


def recurrent_layers(nc, x, state0, wx0, wh0, b0, wx1, wh1, b1, out):
    F32 = mybir.dt.float32
    F16 = mybir.dt.float16
    ALU = mybir.AluOpType
    ACT = mybir.ActivationFunctionType
    AX = mybir.AxisListType

    P = 128
    STEPS = 512
    B = 8
    K = 2
    S = K * B
    PART = 2
    SP = K * PART * B
    CH = 4
    CHUNK = CH * S
    BODY = 2 * CH
    LAG = BODY
    M0, M1 = 8, 6
    IFG = [0, 1, 2, 3, 6, 7]
    OG = [4, 5]

    VS = 64.0
    WS = 64.0
    ACC = VS * WS

    ctx = ExitStack()
    with ctx:
        def sb(name, shape, dt=F32):
            return ctx.enter_context(nc.sbuf_tensor(name, shape, dt))

        def sem(name):
            return ctx.enter_context(nc.semaphore(name))

        xs = sb("xs", [P, STEPS * S])
        stage = sb("stage", [P, 2 * K * (M0 + M1) * P])
        WCOLS = {"wx0": M0 * P, "wh0": M0 * P, "wx1": M1 * P, "wh1": M1 * P}
        wparts = {n: sb(n + "_parts", [P, PART, K, c], F16) for n, c in WCOLS.items()}
        NB = M0 + 8
        bias = sb("bias", [P, NB])
        bias_hi = sb("bias_hi", [P, NB], F16)
        bias_lo = sb("bias_lo", [P, NB], F16)
        bias_mv = sb("bias_mv", [P, NB, CH, PART, B], F16)
        ones = sb("ones", [P, P])
        ident = sb("ident", [P, P], F16)
        cond = sb("cond", [P, S])
        x_parts = sb("x_parts", [P, 2, CH, K, PART, B], F16)
        x1_parts = sb("x1_parts", [P, 2, CH, K, PART, B], F16)
        h0_parts = sb("h0_parts", [P, K, PART, B], F16)
        h1_parts = sb("h1_parts", [P, K, PART, B], F16)
        h0_all = sb("h0_all", [P, BODY, S])
        h1_all = sb("h1_all", [P, BODY, S])
        h1_half = sb("h1_half", [P, S])
        z_ifg = sb("z_ifg", [P, 3 * S])
        z_o = sb("z_o", [P, S])
        cell = sb("cell", [P, 4 * S])
        t_out = sb("t_out", [P, S])
        o_gate = sb("o_gate", [P, S])
        prod = sb("prod", [P, 2 * S])
        t_cell = sb("t_cell", [P, S])
        z_1 = sb("z_1", [P, 3 * S])
        t_1 = sb("t_1", [P, 2 * S])
        gated = sb("gated", [P, S])
        mem = sb("mem", [P, S])
        keep = sb("keep", [P, S])
        fresh = sb("fresh", [P, S])
        t_mem = sb("t_mem", [P, S])
        new = sb("new", [P, S])
        xm = sb("xm", [P, 2, CH, S])

        def bank(name):
            return ctx.enter_context(nc.psum_tensor(name, [P, 512], F32))

        pI = [bank(f"p_ifg{i}") for i in range(2)]
        pO = [bank(f"p_o{i}") for i in range(2)]
        pG = [bank(f"p_gates1_{i}") for i in range(2)]
        pX = [bank(f"p_xm{i}") for i in range(2)]

        def cols(t, tiles):
            return t[:, 0:CH * tiles * PART * B].rearrange("p (t m q b) -> p t m q b", t=CH, m=tiles, q=PART)

        vI, vO = [cols(t, 6) for t in pI], [cols(t, 2) for t in pO]
        vG, vX = [cols(t, 6) for t in pG], [cols(t, 2) for t in pX]

        dma_x0, dma_x, dma_small = sem("dma_x0"), sem("dma_x"), sem("dma_small")
        dma_w = {n: sem("dma_" + n) for n in WCOLS}
        out_stored = sem("out_stored")
        ident_set, ident_ready = sem("ident_set"), sem("ident_ready")
        hi_ready, lo_ready = sem("hi_ready"), sem("lo_ready")
        bias_split, bias_ready = sem("bias_split"), sem("bias_ready")
        state_hi, state_ready = sem("state_hi"), sem("state_ready")
        h0_ready = sem("h0_ready")
        ifg_summed, o_summed = sem("ifg_summed"), sem("o_summed")
        z_ifg_ready, z_o_ready = sem("z_ifg_ready"), sem("z_o_ready")
        ifg_ready, o_ready, cell_tanh = sem("ifg_ready"), sem("o_ready"), sem("cell_tanh")
        prod_ready, cell_ready, o_gate_ready, h0_full = sem("prod_ready"), sem("cell_ready"), sem("o_gate_ready"), sem("h0_full")
        h1_ready = sem("h1_ready")
        g1_summed, z1_ready, t1_ready = sem("g1_summed"), sem("z1_ready"), sem("t1_ready")
        gated_ready, mem_ready, fresh_ready, mem_tanh = sem("gated_ready"), sem("mem_ready"), sem("fresh_ready"), sem("mem_tanh")
        new_ready, h1_full = sem("new_ready"), sem("h1_full")
        x_hi, x_split, x_used = sem("x_hi"), sem("x_split"), sem("x_used")
        x1_ready, x1_hi, x1_split, x1_used = sem("x1_ready"), sem("x1_hi"), sem("x1_split"), sem("x1_used")
        xm_summed, xm_ready, out_ready = sem("xm_summed"), sem("xm_ready"), sem("out_ready")

        STAGE_AT, at = {}, 0
        for n, c in WCOLS.items():
            STAGE_AT[n] = at
            at += K * c

        def staged(n):
            return stage[:, STAGE_AT[n]:STAGE_AT[n] + K * WCOLS[n]].rearrange("p (k c) -> p k c", k=K)

        SPLITS = [
            ("wx0", 0, 3 * K * P, WS / 2), ("wx0", 3 * K * P, 4 * K * P, WS),
            ("wh0", 0, 3 * K * P, WS / 4), ("wh0", 3 * K * P, 4 * K * P, WS / 2),
            ("wx1", 0, 2 * K * P, WS / 2), ("wx1", 2 * K * P, 3 * K * P, WS),
            ("wh1", 0, 3 * K * P, WS / 4),
        ]
        DONE = {n: 1 + max(i for i, s in enumerate(SPLITS) if s[0] == n) for n in WCOLS}

        FIRST = 16
        block = ctx.enter_context(nc.Block())

        LOOP_FROM, LOOP_TO = 2 * BODY, STEPS - BODY

        def slots(eng, slot):
            for t in range(LOOP_FROM):
                slot(0, 0, t)
            with eng.Fori(LOOP_FROM // BODY, LOOP_TO // BODY, 1) as turn:
                base, base_c = eng.snap(turn * BODY), eng.snap(turn * (BODY // CH))
                for t in range(BODY):
                    slot(base, base_c, t)
            for t in range(LOOP_TO, STEPS + LAG + 1):
                slot(0, 0, t)

        def when(base, t):
            return None if not isinstance(base, int) else t

        @block.sync
        def _(sp):
            def rows(a, lo, hi):
                return a[:, lo:hi]

            sp.dma_start(staged("wx0"), wx0).then_inc(dma_w["wx0"], 16)
            sp.dma_start(xs[:, 0:FIRST * S], rows(x, 0, FIRST * S)).then_inc(dma_x0, 16)
            sp.dma_start(staged("wh0"), wh0).then_inc(dma_w["wh0"], 16)
            sp.dma_start(staged("wx1"), wx1).then_inc(dma_w["wx1"], 16)
            sp.dma_start(staged("wh1"), wh1).then_inc(dma_w["wh1"], 16)
            sp.dma_start(xs[:, FIRST * S:], rows(x, FIRST * S, STEPS * S)).then_inc(dma_x, 16)
            W = BODY * S
            with sp.Fori(0, STEPS // BODY, 1) as n:
                sp.wait_ge(out_ready, n * 2 + 2)
                sp.dma_start(out[:, bass.ds(n * W, W)], xs[:, bass.ds(n * W, W)]).then_inc(out_stored, 16)
            sp.wait_ge(out_stored, 16 * (STEPS // BODY))

        @block.gpsimd
        def _(pool):
            pool.dma_start(cond[:, :], state0).then_inc(dma_small, 16)
            pool.dma_start(bias[:, 0:M0], b0).then_inc(dma_small, 16)
            pool.dma_start(bias[:, M0:NB], b1).then_inc(dma_small, 16)
            pool.memset(ones[:, :], WS).then_inc(ident_set, 1)
            pool.wait_ge(ident_set, 1)
            pool.affine_select(out=ident[:, :], in_=ones[:, :], compare_op=ALU.is_equal, fill=0.0,
                               base=0, pattern=[[-1, P]], channel_multiplier=1).then_inc(ident_ready, 1)

        @block.scalar
        def _(act):
            for n, lo, hi, f in SPLITS:
                act.wait_ge(dma_w[n], 16)
                act.activation(wparts[n][:, 0, :, lo:hi], staged(n)[:, :, lo:hi], ACT.Copy, scale=f).then_inc(hi_ready, 1)

            def slot(base, b4, t):
                n = when(base, t)
                u = t - LAG
                if n is None or LAG < n <= STEPS + LAG:
                    act.wait_ge(mem_ready, base + u)
                    act.activation(t_mem[:, :], mem[:, :], ACT.Tanh, scale=1 / ACC).then_inc(mem_tanh, 1)
                if n is None or n < STEPS:
                    act.wait_ge(z_ifg_ready, base + t + 1)
                    act.activation(cell[:, 0:3 * S], z_ifg[:, :], ACT.Tanh, scale=1 / ACC).then_inc(ifg_ready, 1)
                    act.wait_ge(z_o_ready, base + t + 1)
                    act.activation(t_out[:, :], z_o[:, :], ACT.Tanh, scale=1 / ACC).then_inc(o_ready, 1)
                    act.wait_ge(cell_ready, base + t + 1)
                    act.activation(t_cell[:, :], cell[:, 3 * S:4 * S], ACT.Tanh, scale=0.5).then_inc(cell_tanh, 1)
                if n is None or LAG <= n < STEPS + LAG:
                    act.wait_ge(z1_ready, base + u + 1)
                    act.activation(t_1[:, :], z_1[:, 0:2 * S], ACT.Tanh, scale=1 / ACC).then_inc(t1_ready, 1)

            slots(act, slot)

        @block.vector
        def _(dve):
            V = nc.vector

            def parts(t, q):
                return t.rearrange("p k q b -> p q k b")[:, q]

            def split_state(values, dst, full, full_sem, ready):
                raise NotImplementedError

            dve.wait_ge(dma_small, 48)
            V.memset(cell[:, 3 * S:4 * S], 0.0)
            c3 = cond[:, :].rearrange("p (k b) -> p k b", k=K)
            V.tensor_scalar_mul(parts(h0_parts, 0), c3, 2 * VS)
            V.tensor_scalar_mul(parts(h1_parts, 0), c3, 2 * VS)
            V.tensor_scalar_mul(h1_half[:, :], cond[:, :], VS).then_inc(state_hi, 1)
            for lo, hi, f in ((0, 6, WS / 2), (6, 8, WS), (8, 14, WS / 2), (14, 16, WS)):
                ins = V.tensor_scalar_mul(bias_hi[:, lo:hi], bias[:, lo:hi], f)
            ins.then_inc(bias_split, 1)
            dve.wait_ge(state_hi, 1)
            for h in (h0_parts, h1_parts):
                V.scalar_tensor_tensor(out=parts(h, 1), in0=c3, scalar=2 * VS, in1=parts(h, 0),
                                       op0=ALU.mult, op1=ALU.subtract).then_inc(state_ready, 1)
            dve.wait_ge(bias_split, 1)
            for lo, hi, f in ((0, 6, WS / 2), (6, 8, WS), (8, 14, WS / 2), (14, 16, WS)):
                ins = V.scalar_tensor_tensor(out=bias_lo[:, lo:hi], in0=bias[:, lo:hi], scalar=f,
                                             in1=bias_hi[:, lo:hi], op0=ALU.mult, op1=ALU.subtract)
            ins.then_inc(bias_split, 1)
            dve.wait_ge(bias_split, 2)
            for q, src in ((0, bias_hi), (1, bias_lo)):
                for s in range(CH):
                    ins = V.tensor_copy(bias_mv[:, :, s, q, :], src[:, :].unsqueeze(2).to_broadcast([P, NB, B]))
            ins.then_inc(bias_ready, 1)
            def low(i):
                n, lo, hi, f = SPLITS[i]
                dve.wait_ge(hi_ready, i + 1)
                for k in range(K):
                    ins = V.scalar_tensor_tensor(out=wparts[n][:, 1, k, lo:hi], in0=staged(n)[:, k, lo:hi], scalar=f,
                                                 in1=wparts[n][:, 0, k, lo:hi], op0=ALU.mult, op1=ALU.subtract)
                ins.then_inc(lo_ready, 1)

            def chunk_of(c0, c):
                return xs[:, bass.ds(c0 * CHUNK + c * CHUNK, CHUNK)]

            def pair(t, par, q):
                return t[:, par].rearrange("p t k q b -> p q (t k) b")[:, q]

            def x_high(c, b4):
                V.tensor_scalar_mul(pair(x_parts, c % 2, 0), chunk_of(b4, c).rearrange("p (a b) -> p a b", b=B),
                                    VS).then_inc(x_hi, 1)

            def x_low(c, b4):
                dve.wait_ge(x_hi, b4 + c + 1)
                V.scalar_tensor_tensor(out=pair(x_parts, c % 2, 1),
                                       in0=chunk_of(b4, c).rearrange("p (a b) -> p a b", b=B), scalar=VS,
                                       in1=pair(x_parts, c % 2, 0), op0=ALU.mult, op1=ALU.subtract).then_inc(x_split, 1)

            dve.wait_ge(dma_x0, 16)
            for c in range(2):
                x_high(c, 0)
            for c in range(2):
                x_low(c, 0)
            for i in range(len(SPLITS)):
                low(i)
            dve.wait_ge(dma_x, 16)

            def slot(base, b4, t):
                n = when(base, t)
                u = t - LAG
                i0, i1 = t % BODY, (t - 1) % BODY
                c, tt = t // CH, t % CH
                l0 = n is None or n < STEPS

                if n is None or LAG < n <= STEPS + LAG:
                    dve.wait_ge(mem_tanh, base + u)
                    dve.wait_ge(fresh_ready, base + u)
                    V.tensor_tensor(new[:, :], fresh[:, :], t_mem[:, :], ALU.mult).then_inc(new_ready, 1)
                    dve.wait_ge(new_ready, base + u)
                    n3 = new[:, :].rearrange("p (k b) -> p k b", k=K)
                    k3 = keep[:, :].rearrange("p (k b) -> p k b", k=K)
                    V.tensor_tensor(parts(h1_parts, 0), n3, k3, ALU.add)
                    V.tensor_tensor(h1_all[:, i1, :], new[:, :], keep[:, :], ALU.add).then_inc(h1_full, 1)
                    dve.wait_ge(h1_full, base + u)
                    a3 = h1_all[:, i1, :].rearrange("p (k b) -> p k b", k=K)
                    V.tensor_tensor(parts(h1_parts, 1), a3, parts(h1_parts, 0), ALU.subtract).then_inc(h1_ready, 1)
                    V.tensor_scalar_mul(h1_half[:, :], h1_all[:, i1, :], 0.5)

                if l0:
                    dve.wait_ge(ifg_summed, base + t + 1)
                    V.tensor_reduce(z_ifg[:, :].rearrange("p (m b) -> p m b", b=B),
                                    vI[c % 2][:, tt].rearrange("p m q b -> p m b q"), AX.X, ALU.add).then_inc(z_ifg_ready, 1)
                    dve.wait_ge(o_summed, base + t + 1)
                    V.tensor_reduce(z_o[:, :].rearrange("p (m b) -> p m b", b=B),
                                    vO[c % 2][:, tt].rearrange("p m q b -> p m b q"), AX.X, ALU.add).then_inc(z_o_ready, 1)
                    dve.wait_ge(ifg_ready, base + t + 1)
                    V.scalar_tensor_tensor(out=prod[:, :], in0=cell[:, 0:2 * S], scalar=1.0, in1=cell[:, 2 * S:4 * S],
                                           op0=ALU.add, op1=ALU.mult).then_inc(prod_ready, 1)
                    dve.wait_ge(prod_ready, base + t + 1)
                    V.scalar_tensor_tensor(out=cell[:, 3 * S:4 * S], in0=prod[:, S:2 * S], scalar=0.5, in1=prod[:, 0:S],
                                           op0=ALU.mult, op1=ALU.add).then_inc(cell_ready, 1)
                if n is None or LAG <= n < STEPS + LAG:
                    dve.wait_ge(g1_summed, base + u + 1)
                    V.tensor_reduce(z_1[:, :].rearrange("p (m b) -> p m b", b=B),
                                    vG[(c + LAG // CH) % 2][:, tt].rearrange("p m q b -> p m b q"), AX.X,
                                    ALU.add).then_inc(z1_ready, 1)
                if l0:
                    dve.wait_ge(o_ready, base + t + 1)
                    V.tensor_scalar(o_gate[:, :], t_out[:, :], VS, VS, ALU.mult, ALU.add).then_inc(o_gate_ready, 1)
                    dve.wait_ge(cell_tanh, base + t + 1)
                    dve.wait_ge(o_gate_ready, base + t + 1)
                    V.tensor_tensor(parts(h0_parts, 0), o_gate[:, :].rearrange("p (k b) -> p k b", k=K),
                                    t_cell[:, :].rearrange("p (k b) -> p k b", k=K), ALU.mult)
                    V.tensor_tensor(h0_all[:, i0, :], o_gate[:, :], t_cell[:, :], ALU.mult).then_inc(h0_full, 1)
                    dve.wait_ge(h0_full, base + t + 1)
                    V.tensor_tensor(parts(h0_parts, 1), h0_all[:, i0, :].rearrange("p (k b) -> p k b", k=K),
                                    parts(h0_parts, 0), ALU.subtract).then_inc(h0_ready, 1)
                if n is None or LAG <= n < STEPS + LAG:
                    dve.wait_ge(t1_ready, base + u + 1)
                    V.scalar_tensor_tensor(out=gated[:, :], in0=t_1[:, 0:S], scalar=1.0, in1=z_1[:, 2 * S:3 * S],
                                           op0=ALU.add, op1=ALU.mult).then_inc(gated_ready, 1)
                    dve.wait_ge(gated_ready, base + u + 1)
                    if tt == 0:
                        dve.wait_ge(xm_ready, b4 + c - 1)
                    V.tensor_tensor(mem[:, :], gated[:, :], xm[:, c % 2, tt, :], ALU.add).then_inc(mem_ready, 1)
                    V.scalar_tensor_tensor(out=keep[:, :], in0=t_1[:, S:2 * S], scalar=1.0, in1=h1_half[:, :],
                                           op0=ALU.add, op1=ALU.mult)
                    V.tensor_scalar(fresh[:, :], t_1[:, S:2 * S], -VS, VS, ALU.mult, ALU.add).then_inc(fresh_ready, 1)

                more_x = n is None or c + 2 < STEPS // CH
                if tt == 0 and more_x:
                    dve.wait_ge(x_used, b4 + c + 1)
                    x_high(c + 2, b4)
                if tt == 1 and more_x:
                    x_low(c + 2, b4)
                if n is None or 1 <= c <= STEPS // CH:
                    here = chunk_of(b4, c - 1)
                    if tt == 0:
                        V.scalar_tensor_tensor(out=here, in0=h0_all[:, ((c - 1) % 2) * CH:((c - 1) % 2 + 1) * CH, :].rearrange("p t s -> p (t s)"),
                                               scalar=1 / (2 * VS), in1=here, op0=ALU.mult, op1=ALU.add).then_inc(x1_ready, 1)
                        dve.wait_ge(x1_ready, b4 + c)
                        if n is None or c > 2:
                            dve.wait_ge(x1_used, b4 + c - 2)
                        V.tensor_scalar_mul(pair(x1_parts, (c - 1) % 2, 0), here.rearrange("p (a b) -> p a b", b=B),
                                            VS).then_inc(x1_hi, 1)
                    if tt == 1:
                        dve.wait_ge(x1_hi, b4 + c)
                        V.scalar_tensor_tensor(out=pair(x1_parts, (c - 1) % 2, 1), in0=here.rearrange("p (a b) -> p a b", b=B),
                                               scalar=VS, in1=pair(x1_parts, (c - 1) % 2, 0), op0=ALU.mult,
                                               op1=ALU.subtract).then_inc(x1_split, 1)
                    if tt == 3:
                        dve.wait_ge(xm_summed, b4 + c)
                        V.tensor_reduce(xm[:, (c - 1) % 2].rearrange("p t (m b) -> p (t m) b", b=B),
                                        vX[(c - 1) % 2].rearrange("p t m q b -> p (t m) b q"), AX.X, ALU.add).then_inc(xm_ready, 1)
                last = n is not None and n == STEPS + LAG
                if (tt == 3 and (n is None or 3 <= c)) or last:
                    d = c - 3
                    here = chunk_of(b4, d)
                    V.scalar_tensor_tensor(out=here, in0=h1_all[:, (d % 2) * CH:(d % 2 + 1) * CH, :].rearrange("p t s -> p (t s)"),
                                           scalar=1 / (2 * VS), in1=here, op0=ALU.mult, op1=ALU.add).then_inc(out_ready, 1)

            slots(dve, slot)

        @block.tensor
        def _(pe):
            def mm(o, w, m, rhs, start=False):
                return nc.tensor.matmul(o, w, rhs, start=start, stop=True, skip_group_check=True)

            def tile(n, q, k, m):
                return wparts[n][:, q, k, m * P:(m + 1) * P]

            def xbias(o, col, start):
                return mm(o, ident[:, :], 0, bias_mv[:, col].rearrange("p t q b -> p t (q b)"), start)

            def chunk_cols(v, m):
                return v[:, :, m].rearrange("p t q b -> p t (q b)")

            def input_work(c):
                par = c % 2
                out_of = [(vI[par], j, m) for j, m in enumerate(IFG)] + [(vO[par], j, m) for j, m in enumerate(OG)]
                for v, j, m in out_of:
                    yield lambda v=v, j=j, m=m: xbias(chunk_cols(v, j), m, j == 0)
                    for q in range(PART):
                        for k in range(K):
                            yield lambda v=v, j=j, m=m, q=q, k=k: mm(
                                chunk_cols(v, j), tile("wx0", q, k, m), m,
                                x_parts[:, par, :, k].rearrange("p t q b -> p t (q b)"))

            def input_work_1(c, tiles):
                par = c % 2
                for what, j in tiles:
                    v = vX[par] if what == "xm" else vG[par]
                    col = M0 + 6 + j if what == "xm" else M0 + j
                    yield lambda v=v, j=j, col=col: xbias(chunk_cols(v, j), col, j == 0)
                    if what == "hW":
                        continue
                    m = 4 + j if what == "xm" else j
                    for q in range(PART):
                        for k in range(K):
                            yield lambda v=v, j=j, m=m, q=q, k=k: mm(
                                chunk_cols(v, j), tile("wx1", q, k, m), m,
                                x1_parts[:, par, :, k].rearrange("p t q b -> p t (q b)"))

            XM = [("xm", 0), ("xm", 1)]
            G1 = [("gates", 0), ("gates", 1), ("gates", 2), ("gates", 3), ("hW", 4), ("hW", 5)]

            def issue(work):
                ins = None
                for w in work:
                    ins = w()
                return ins

            def recurrent(v, tiles, n, h):
                for j, m in enumerate(tiles):
                    for q in range(PART):
                        for k in range(K):
                            ins = mm(v[:, j].rearrange("p q b -> p (q b)"), tile(n, q, k, m), m,
                                     h[:, k].rearrange("p q b -> p (q b)"))
                return ins

            pe.wait_ge(ident_ready, 1)
            pe.wait_ge(bias_ready, 1)
            pe.wait_ge(hi_ready, DONE["wx0"])
            pe.wait_ge(lo_ready, DONE["wx0"])
            pe.wait_ge(x_split, 1)
            issue(input_work(0)).then_inc(x_used, 1)
            pe.wait_ge(hi_ready, len(SPLITS))
            pe.wait_ge(lo_ready, len(SPLITS))
            pe.wait_ge(state_ready, 2)

            def slot(base, b4, t):
                n = when(base, t)
                u = t - LAG
                c, tt = t // CH, t % CH
                if n is None or n < STEPS:
                    if n != 0:
                        pe.wait_ge(h0_ready, base + t)
                    recurrent(vI[c % 2][:, tt], IFG, "wh0", h0_parts).then_inc(ifg_summed, 1)
                    recurrent(vO[c % 2][:, tt], OG, "wh0", h0_parts).then_inc(o_summed, 1)
                if n is None or LAG <= n < STEPS + LAG:
                    if n != LAG:
                        pe.wait_ge(h1_ready, base + u)
                    recurrent(vG[c % 2][:, tt], range(M1), "wh1", h1_parts).then_inc(g1_summed, 1)
                if n is None or c + 1 < STEPS // CH:
                    work = list(input_work(c + 1))
                    if tt == 0:
                        pe.wait_ge(x_split, b4 + c + 2)
                        issue(work[:20])
                    if tt == 1:
                        issue(work[20:]).then_inc(x_used, 1)
                if n is None or 1 <= c <= STEPS // CH:
                    if tt == 2:
                        pe.wait_ge(x1_split, b4 + c)
                        if n is None or c > 2:
                            pe.wait_ge(xm_ready, b4 + c - 2)
                        issue(input_work_1(c - 1, XM)).then_inc(xm_summed, 1)
                        issue(input_work_1(c - 1, G1[:2]))
                    if tt == 3:
                        issue(input_work_1(c - 1, G1[2:])).then_inc(x1_used, 1)

            slots(pe, slot)


def kernel(x, cond_1024, L0_cond_Wx, L0_cond_Wh, L0_cond_b, L1_cond_w_W, L1_cond_w_b,
           L1_cond_wx_W, L1_cond_wx_b, L1_cond_wh_W, L1_cond_wh_b):
    import numpy as np
    import concourse.bacc as bacc
    from concourse import mybir as _mybir
    from concourse.bass_utils import run_bass_kernel_spmd

    n, steps, d = x.shape
    p, k = 128, d // 128

    def matrix(w):
        w = np.asarray(w)
        return np.ascontiguousarray(w.reshape(k, p, -1).transpose(1, 0, 2))

    def column(b):
        return np.asarray(b).reshape(-1, p).T

    w_W = np.asarray(L1_cond_w_W)
    arrays = {
        "x": np.ascontiguousarray(np.asarray(x).reshape(n, steps, k, p).transpose(3, 1, 2, 0)).reshape(p, -1),
        "state0": np.ascontiguousarray(np.asarray(cond_1024).reshape(n, k, p).transpose(2, 1, 0)).reshape(p, -1),
        "wx0": matrix(L0_cond_Wx), "wh0": matrix(L0_cond_Wh),
        "b0": np.ascontiguousarray(column(L0_cond_b)),
        "wx1": matrix(np.concatenate([w_W[:d], np.asarray(L1_cond_wx_W)], axis=1)),
        "wh1": matrix(np.concatenate([w_W[d:], np.asarray(L1_cond_wh_W)], axis=1)),
        "b1": np.ascontiguousarray(np.concatenate(
            [column(L1_cond_w_b), column(L1_cond_wh_b), column(L1_cond_wx_b)], axis=1)),
    }
    nc = bacc.Bacc("TRN2", target_bir_lowering=False, num_devices=1)
    args = [nc.dram_tensor(name, a.shape, _mybir.dt.float32, kind="ExternalInput").ap() for name, a in arrays.items()]
    out = nc.dram_tensor("out", [p, steps * k * n], _mybir.dt.float32, kind="ExternalOutput").ap()
    recurrent_layers(nc, *args, out)
    r = run_bass_kernel_spmd(nc, [arrays], core_ids=[0])
    got = np.asarray(r.results[0]["out"]).reshape(p, steps, k, n)
    return np.ascontiguousarray(got.transpose(3, 1, 2, 0)).reshape(n, steps, d)
```

```python
import concourse.bass as bass
from concourse import mybir
from contextlib import ExitStack


def recurrent_layers(nc, x, state0, wx0, wh0, b0, wx1, wh1, b1, out):
    F32 = mybir.dt.float32
    F16 = mybir.dt.float16
    ALU = mybir.AluOpType
    ACT = mybir.ActivationFunctionType
    AX = mybir.AxisListType

    P = 128
    STEPS = 512
    B = 8
    K = 2
    S = K * B
    PART = 2
    SP = K * PART * B
    CH = 4
    CHUNK = CH * S
    BODY = 2 * CH
    LAG = BODY
    M0, M1 = 8, 6
    GI, F, O = [6, 7, 0, 1], [2, 3], [4, 5]
    HID, OUT, CAND, MEM = [0, 1], [2, 3], [4, 5], [4, 5]

    VS = 64.0
    WS = 64.0
    ACC = VS * WS

    ctx = ExitStack()
    with ctx:
        def sb(name, shape, dt=F32):
            return ctx.enter_context(nc.sbuf_tensor(name, shape, dt))

        def sem(name):
            return ctx.enter_context(nc.semaphore(name))

        xs = sb("xs", [P, STEPS * S])
        stage = sb("stage", [P, 2 * K * (M0 + M1) * P])
        WCOLS = {"wx0": M0 * P, "wh0": M0 * P, "wx1": M1 * P, "wh1": M1 * P}
        wparts = {n: sb(n + "_parts", [P, PART, K, c], F16) for n, c in WCOLS.items()}
        NB = M0 + 8
        bias = sb("bias", [P, NB])
        bias_hi = sb("bias_hi", [P, NB], F16)
        bias_lo = sb("bias_lo", [P, NB], F16)
        bias_mv = sb("bias_mv", [P, NB, CH, PART, B], F16)
        ones = sb("ones", [P, P])
        ident = sb("ident", [P, P], F16)
        cond = sb("cond", [P, S])
        x_parts = sb("x_parts", [P, 2, CH, K, PART, B], F16)
        x1_parts = sb("x1_parts", [P, 2, CH, K, PART, B], F16)
        h0_parts = sb("h0_parts", [P, K, PART, B], F16)
        h1_parts = sb("h1_parts", [P, K, PART, B], F16)
        h0_all = sb("h0_all", [P, BODY, S])
        h1_all = sb("h1_all", [P, BODY, S])
        h1_half = sb("h1_half", [P, S])
        z_gi = sb("z_gi", [P, 2 * S])
        z_f = sb("z_f", [P, S])
        z_o = sb("z_o", [P, S])
        gi = sb("gi", [P, 2 * S])
        t_f = sb("t_f", [P, S])
        t_o = sb("t_o", [P, S])
        o_gate = sb("o_gate", [P, S])
        added = sb("added", [P, S])
        kept = sb("kept", [P, S])
        cell = sb("cell", [P, S])
        t_cell = sb("t_cell", [P, S])
        z_hid = sb("z_hid", [P, S])
        z_cand = sb("z_cand", [P, S])
        z_out = sb("z_out", [P, S])
        t_hid = sb("t_hid", [P, S])
        t_out = sb("t_out", [P, S])
        gated = sb("gated", [P, S])
        mem = sb("mem", [P, S])
        keep = sb("keep", [P, S])
        fresh = sb("fresh", [P, S])
        t_mem = sb("t_mem", [P, S])
        new = sb("new", [P, S])
        xm = sb("xm", [P, 2, CH, S])

        def bank(name):
            return ctx.enter_context(nc.psum_tensor(name, [P, 512], F32))

        WIDTH = CH * PART * B
        b_gi = [bank(f"b_gi_out_mem{i}") for i in range(2)]
        b_f = [bank(f"b_f_cand{i}") for i in range(2)]
        b_o = [bank(f"b_o{i}") for i in range(2)]
        b_hid = [bank(f"b_hid{i}") for i in range(2)]

        def cols(banks, first, tiles):
            return [t[:, first * WIDTH:(first + tiles) * WIDTH]
                    .rearrange("p (t m q b) -> p t m q b", t=CH, m=tiles, q=PART) for t in banks]

        s_gi, s_out, s_mem = cols(b_gi, 0, 4), cols(b_gi, 4, 2), cols(b_gi, 6, 2)
        s_f, s_cand = cols(b_f, 0, 2), cols(b_f, 2, 2)
        s_o, s_hid = cols(b_o, 0, 2), cols(b_hid, 0, 2)

        dma_x0, dma_x, dma_small = sem("dma_x0"), sem("dma_x"), sem("dma_small")
        dma_w = {n: sem("dma_" + n) for n in WCOLS}
        out_stored = sem("out_stored")
        ident_set, ident_ready = sem("ident_set"), sem("ident_ready")
        hi_ready, lo_ready = sem("hi_ready"), sem("lo_ready")
        bias_split, bias_ready = sem("bias_split"), sem("bias_ready")
        state_hi, state_ready = sem("state_hi"), sem("state_ready")
        h0_ready, h0_whole = sem("h0_ready"), sem("h0_whole")
        gi_summed, f_summed, o_summed = sem("gi_summed"), sem("f_summed"), sem("o_summed")
        z_gi_ready, z_f_ready, z_o_ready = sem("z_gi_ready"), sem("z_f_ready"), sem("z_o_ready")
        gi_ready, f_ready, t_o_ready, cell_tanh = sem("gi_ready"), sem("f_ready"), sem("t_o_ready"), sem("cell_tanh")
        kept_ready, cell_ready = sem("kept_ready"), sem("cell_ready")
        h1_ready, h1_whole = sem("h1_ready"), sem("h1_whole")
        hid_summed, cand_summed, out_summed = sem("hid_summed"), sem("cand_summed"), sem("out_summed")
        z_hid_ready, z_cand_ready, z_out_ready = sem("z_hid_ready"), sem("z_cand_ready"), sem("z_out_ready")
        t_hid_ready, t_out_ready, mem_tanh = sem("t_hid_ready"), sem("t_out_ready"), sem("mem_tanh")
        gated_ready, mem_ready, new_ready = sem("gated_ready"), sem("mem_ready"), sem("new_ready")
        x_hi, x_split, x_used = sem("x_hi"), sem("x_split"), sem("x_used")
        x1_ready, x1_hi, x1_split, x1_used = sem("x1_ready"), sem("x1_hi"), sem("x1_split"), sem("x1_used")
        mem_summed, xm_ready, out_ready = sem("mem_summed"), sem("xm_ready"), sem("out_ready")

        STAGE_AT, at = {}, 0
        for n, c in WCOLS.items():
            STAGE_AT[n] = at
            at += K * c

        def staged(n):
            return stage[:, STAGE_AT[n]:STAGE_AT[n] + K * WCOLS[n]].rearrange("p (k c) -> p k c", k=K)

        SPLITS = [
            ("wx0", 0, 3 * K * P, WS / 2), ("wx0", 3 * K * P, 4 * K * P, WS),
            ("wh0", 0, 3 * K * P, WS / 4), ("wh0", 3 * K * P, 4 * K * P, WS / 2),
            ("wx1", 0, 2 * K * P, WS / 2), ("wx1", 2 * K * P, 3 * K * P, WS),
            ("wh1", 0, 3 * K * P, WS / 4),
        ]
        DONE = {n: 1 + max(i for i, s in enumerate(SPLITS) if s[0] == n) for n in WCOLS}

        FIRST = 16
        block = ctx.enter_context(nc.Block())

        LOOP_FROM, LOOP_TO = 2 * BODY, STEPS - BODY

        def slots(eng, slot):
            for t in range(LOOP_FROM):
                slot(0, 0, t)
            with eng.Fori(LOOP_FROM // BODY, LOOP_TO // BODY, 1) as turn:
                base, base_c = eng.snap(turn * BODY), eng.snap(turn * (BODY // CH))
                for t in range(BODY):
                    slot(base, base_c, t)
            for t in range(LOOP_TO, STEPS + LAG + 1):
                slot(0, 0, t)

        def when(base, t):
            return None if not isinstance(base, int) else t

        def chunk_of(c0, c):
            return xs[:, bass.ds(c0 * CHUNK + c * CHUNK, CHUNK)]

        def pair(t, par, q):
            return t[:, par].rearrange("p t k q b -> p q (t k) b")[:, q]

        @block.sync
        def _(sp):
            def rows(a, lo, hi):
                return a[:, lo:hi]

            sp.dma_start(staged("wx0"), wx0).then_inc(dma_w["wx0"], 16)
            sp.dma_start(xs[:, 0:FIRST * S], rows(x, 0, FIRST * S)).then_inc(dma_x0, 16)
            sp.dma_start(staged("wh0"), wh0).then_inc(dma_w["wh0"], 16)
            sp.dma_start(staged("wx1"), wx1).then_inc(dma_w["wx1"], 16)
            sp.dma_start(staged("wh1"), wh1).then_inc(dma_w["wh1"], 16)
            sp.dma_start(xs[:, FIRST * S:], rows(x, FIRST * S, STEPS * S)).then_inc(dma_x, 16)
            W = BODY * S
            with sp.Fori(0, STEPS // BODY, 1) as n:
                sp.wait_ge(out_ready, n * 2 + 2)
                sp.dma_start(out[:, bass.ds(n * W, W)], xs[:, bass.ds(n * W, W)]).then_inc(out_stored, 16)
            sp.wait_ge(out_stored, 16 * (STEPS // BODY))

        @block.gpsimd
        def _(pool):
            pool.dma_start(cond[:, :], state0).then_inc(dma_small, 16)
            pool.dma_start(bias[:, 0:M0], b0).then_inc(dma_small, 16)
            pool.dma_start(bias[:, M0:NB], b1).then_inc(dma_small, 16)
            pool.memset(ones[:, :], WS).then_inc(ident_set, 1)
            pool.wait_ge(ident_set, 1)
            pool.affine_select(out=ident[:, :], in_=ones[:, :], compare_op=ALU.is_equal, fill=0.0,
                               base=0, pattern=[[-1, P]], channel_multiplier=1).then_inc(ident_ready, 1)

        @block.scalar
        def _(act):
            def x_high(c, b4):
                act.activation(pair(x_parts, c % 2, 0), chunk_of(b4, c).rearrange("p (a b) -> p a b", b=B),
                               ACT.Copy, scale=VS).then_inc(x_hi, 1)

            act.wait_ge(dma_x0, 16)
            for c in range(2):
                x_high(c, 0)
            for n, lo, hi, f in SPLITS:
                act.wait_ge(dma_w[n], 16)
                act.activation(wparts[n][:, 0, :, lo:hi], staged(n)[:, :, lo:hi], ACT.Copy, scale=f).then_inc(hi_ready, 1)

            def tanh(out_, in_, scale, done):
                act.activation(out_[:, :], in_[:, :], ACT.Tanh, scale=scale).then_inc(done, 1)

            def slot(base, b4, t):
                n = when(base, t)
                u = t - LAG
                c, tt = t // CH, t % CH
                l0 = n is None or n < STEPS
                l1 = n is None or LAG <= n < STEPS + LAG
                if l0:
                    act.wait_ge(z_gi_ready, base + t + 1)
                    tanh(gi, z_gi, 1 / ACC, gi_ready)
                    act.wait_ge(z_f_ready, base + t + 1)
                    tanh(t_f, z_f, 1 / ACC, f_ready)
                    act.wait_ge(z_o_ready, base + t + 1)
                    tanh(t_o, z_o, 1 / ACC, t_o_ready)
                    act.wait_ge(t_o_ready, base + t + 1)
                    act.activation(o_gate[:, :], t_o[:, :], ACT.Copy, bias=VS, scale=VS)
                if l1:
                    act.wait_ge(z_hid_ready, base + u + 1)
                    tanh(t_hid, z_hid, 1 / ACC, t_hid_ready)
                if l0:
                    act.wait_ge(cell_ready, base + t + 1)
                    tanh(t_cell, cell, 0.5, cell_tanh)
                if l1:
                    if n is None or n > LAG:
                        act.wait_ge(h1_whole, base + u)
                        act.activation(h1_half[:, :], h1_all[:, (t - 1) % BODY, :], ACT.Copy, scale=0.5)
                    act.wait_ge(z_out_ready, base + u + 1)
                    tanh(t_out, z_out, 1 / ACC, t_out_ready)
                    act.wait_ge(t_out_ready, base + u + 1)
                    act.activation(fresh[:, :], t_out[:, :], ACT.Copy, bias=VS, scale=-VS)
                if l1:
                    act.wait_ge(mem_ready, base + u + 1)
                    tanh(t_mem, mem, 1 / ACC, mem_tanh)
                if tt == 1 and (n is None or c + 2 < STEPS // CH):
                    act.wait_ge(x_used, b4 + c + 1)
                    x_high(c + 2, b4)
                if tt == 0 and (n is None or 1 <= c <= STEPS // CH):
                    if n is None or c > 2:
                        act.wait_ge(x1_used, b4 + c - 2)
                    act.wait_ge(x1_ready, b4 + c)
                    act.activation(pair(x1_parts, (c - 1) % 2, 0), chunk_of(b4, c - 1).rearrange("p (a b) -> p a b", b=B),
                                   ACT.Copy, scale=VS).then_inc(x1_hi, 1)

            slots(act, slot)

        @block.vector
        def _(dve):
            V = nc.vector

            def parts(t, q):
                return t.rearrange("p k q b -> p q k b")[:, q]

            def add_parts(z, sums, done):
                V.tensor_reduce(z.rearrange("p (m b) -> p m b", b=B), sums.rearrange("p m q b -> p m b q"),
                                AX.X, ALU.add).then_inc(done, 1)

            def heads(t):
                return t.rearrange("p (k b) -> p k b", k=K)

            def steps_of(t, c):
                first = (c % 2) * CH
                return t[:, first:first + CH, :].rearrange("p t s -> p (t s)")

            def one_plus(o, t, by, done=None):
                ins = V.scalar_tensor_tensor(out=o[:, :], in0=t, scalar=1.0, in1=by, op0=ALU.add, op1=ALU.mult)
                if done is not None:
                    ins.then_inc(done, 1)

            dve.wait_ge(dma_small, 48)
            V.memset(cell[:, :], 0.0)
            c3 = cond[:, :].rearrange("p (k b) -> p k b", k=K)
            V.tensor_scalar_mul(parts(h0_parts, 0), c3, 2 * VS)
            V.tensor_scalar_mul(parts(h1_parts, 0), c3, 2 * VS)
            V.tensor_scalar_mul(h1_half[:, :], cond[:, :], VS).then_inc(state_hi, 1)
            for lo, hi, f in ((0, 6, WS / 2), (6, 8, WS), (8, 14, WS / 2), (14, 16, WS)):
                ins = V.tensor_scalar_mul(bias_hi[:, lo:hi], bias[:, lo:hi], f)
            ins.then_inc(bias_split, 1)
            dve.wait_ge(state_hi, 1)
            for h in (h0_parts, h1_parts):
                V.scalar_tensor_tensor(out=parts(h, 1), in0=c3, scalar=2 * VS, in1=parts(h, 0),
                                       op0=ALU.mult, op1=ALU.subtract).then_inc(state_ready, 1)
            dve.wait_ge(bias_split, 1)
            for lo, hi, f in ((0, 6, WS / 2), (6, 8, WS), (8, 14, WS / 2), (14, 16, WS)):
                ins = V.scalar_tensor_tensor(out=bias_lo[:, lo:hi], in0=bias[:, lo:hi], scalar=f,
                                             in1=bias_hi[:, lo:hi], op0=ALU.mult, op1=ALU.subtract)
            ins.then_inc(bias_split, 1)
            dve.wait_ge(bias_split, 2)
            for q, src in ((0, bias_hi), (1, bias_lo)):
                for s in range(CH):
                    ins = V.tensor_copy(bias_mv[:, :, s, q, :], src[:, :].unsqueeze(2).to_broadcast([P, NB, B]))
            ins.then_inc(bias_ready, 1)
            def low(i):
                n, lo, hi, f = SPLITS[i]
                dve.wait_ge(hi_ready, i + 1)
                for k in range(K):
                    ins = V.scalar_tensor_tensor(out=wparts[n][:, 1, k, lo:hi], in0=staged(n)[:, k, lo:hi], scalar=f,
                                                 in1=wparts[n][:, 0, k, lo:hi], op0=ALU.mult, op1=ALU.subtract)
                ins.then_inc(lo_ready, 1)

            def x_low(c, b4):
                dve.wait_ge(x_hi, b4 + c + 1)
                V.scalar_tensor_tensor(out=pair(x_parts, c % 2, 1),
                                       in0=chunk_of(b4, c).rearrange("p (a b) -> p a b", b=B), scalar=VS,
                                       in1=pair(x_parts, c % 2, 0), op0=ALU.mult, op1=ALU.subtract).then_inc(x_split, 1)

            dve.wait_ge(dma_x0, 16)
            for c in range(2):
                x_low(c, 0)
            for i in range(len(SPLITS)):
                low(i)
            dve.wait_ge(dma_x, 16)

            def slot(base, b4, t):
                n = when(base, t)
                u = t - LAG
                i0 = t % BODY
                c, tt = t // CH, t % CH
                l0 = n is None or n < STEPS
                l1 = n is None or LAG <= n < STEPS + LAG
                more_x = n is None or c + 2 < STEPS // CH
                have_x1 = n is None or 1 <= c <= STEPS // CH
                g0, g1 = c % 2, (c - LAG // CH) % 2

                if l0:
                    dve.wait_ge(gi_summed, base + t + 1)
                    add_parts(z_gi[:, :], s_gi[g0][:, tt], z_gi_ready)
                    dve.wait_ge(f_summed, base + t + 1)
                    add_parts(z_f[:, :], s_f[g0][:, tt], z_f_ready)

                here = chunk_of(b4, c - 1) if have_x1 else None
                if tt == 0 and have_x1:
                    V.scalar_tensor_tensor(out=here, in0=steps_of(h0_all, c - 1), scalar=1 / (2 * VS), in1=here,
                                           op0=ALU.mult, op1=ALU.add).then_inc(x1_ready, 1)
                if tt == 1 and have_x1:
                    dve.wait_ge(x1_hi, b4 + c)
                    V.scalar_tensor_tensor(out=pair(x1_parts, (c - 1) % 2, 1), in0=here.rearrange("p (a b) -> p a b", b=B),
                                           scalar=VS, in1=pair(x1_parts, (c - 1) % 2, 0), op0=ALU.mult,
                                           op1=ALU.subtract).then_inc(x1_split, 1)
                if tt == 2 and more_x:
                    x_low(c + 2, b4)
                if (tt == 3 and (n is None or 3 <= c)) or (n is not None and n == STEPS + LAG):
                    result = chunk_of(b4, c - 3)
                    V.scalar_tensor_tensor(out=result, in0=steps_of(h1_all, c - 3), scalar=1 / (2 * VS), in1=result,
                                           op0=ALU.mult, op1=ALU.add).then_inc(out_ready, 1)

                if l0:
                    dve.wait_ge(o_summed, base + t + 1)
                    add_parts(z_o[:, :], s_o[g0][:, tt], z_o_ready)
                    dve.wait_ge(gi_ready, base + t + 1)
                    one_plus(added, gi[:, S:2 * S], gi[:, 0:S])
                    dve.wait_ge(f_ready, base + t + 1)
                    one_plus(kept, t_f[:, :], cell[:, :], kept_ready)
                if l1:
                    dve.wait_ge(hid_summed, base + u + 1)
                    add_parts(z_hid[:, :], s_hid[g1][:, tt], z_hid_ready)
                if l0:
                    dve.wait_ge(kept_ready, base + t + 1)
                    V.scalar_tensor_tensor(out=cell[:, :], in0=kept[:, :], scalar=0.5, in1=added[:, :],
                                           op0=ALU.mult, op1=ALU.add).then_inc(cell_ready, 1)
                if l1:
                    dve.wait_ge(cand_summed, base + u + 1)
                    add_parts(z_cand[:, :], s_cand[g1][:, tt], z_cand_ready)
                    dve.wait_ge(z_cand_ready, base + u + 1)
                    dve.wait_ge(out_summed, base + u + 1)
                    add_parts(z_out[:, :], s_out[g1][:, tt], z_out_ready)
                    dve.wait_ge(t_hid_ready, base + u + 1)
                    one_plus(gated, t_hid[:, :], z_cand[:, :], gated_ready)
                if l0:
                    dve.wait_ge(cell_tanh, base + t + 1)
                    V.tensor_tensor(parts(h0_parts, 0), heads(o_gate[:, :]), heads(t_cell[:, :]), ALU.mult)
                    V.tensor_tensor(h0_all[:, i0, :], o_gate[:, :], t_cell[:, :], ALU.mult).then_inc(h0_whole, 1)
                if l1:
                    dve.wait_ge(gated_ready, base + u + 1)
                    V.tensor_tensor(mem[:, :], gated[:, :], xm[:, c % 2, tt, :], ALU.add).then_inc(mem_ready, 1)
                if l0:
                    dve.wait_ge(h0_whole, base + t + 1)
                    V.tensor_tensor(parts(h0_parts, 1), heads(h0_all[:, i0, :]), parts(h0_parts, 0),
                                    ALU.subtract).then_inc(h0_ready, 1)
                if l1:
                    dve.wait_ge(t_out_ready, base + u + 1)
                    one_plus(keep, t_out[:, :], h1_half[:, :])

                if tt == 2 and have_x1:
                    dve.wait_ge(mem_summed, b4 + c)
                    V.tensor_reduce(xm[:, (c - 1) % 2].rearrange("p t (m b) -> p (t m) b", b=B),
                                    s_mem[(c - 1) % 2].rearrange("p t m q b -> p (t m) b q"), AX.X, ALU.add).then_inc(xm_ready, 1)
                if l1:
                    dve.wait_ge(mem_tanh, base + u + 1)
                    V.tensor_tensor(new[:, :], fresh[:, :], t_mem[:, :], ALU.mult).then_inc(new_ready, 1)
                    dve.wait_ge(new_ready, base + u + 1)
                    V.tensor_tensor(parts(h1_parts, 0), heads(new[:, :]), heads(keep[:, :]), ALU.add)
                    V.tensor_tensor(h1_all[:, i0, :], new[:, :], keep[:, :], ALU.add).then_inc(h1_whole, 1)
                    dve.wait_ge(h1_whole, base + u + 1)
                    V.tensor_tensor(parts(h1_parts, 1), heads(h1_all[:, i0, :]), parts(h1_parts, 0),
                                    ALU.subtract).then_inc(h1_ready, 1)

            slots(dve, slot)

        @block.tensor
        def _(pe):
            def mm(o, w, rhs, start=False):
                return nc.tensor.matmul(o, w, rhs, start=start, stop=True, skip_group_check=True)

            def tile(n, q, k, m):
                return wparts[n][:, q, k, m * P:(m + 1) * P]

            def first_layer(par):
                return [(s_gi[par], j, "gi", m, m) for j, m in enumerate(GI)] + \
                       [(s_f[par], j, "f", m, m) for j, m in enumerate(F)] + \
                       [(s_o[par], j, "o", m, m) for j, m in enumerate(O)]

            def second_layer(par):
                return [(s_mem[par], j, "gi", m, M0 + 6 + j) for j, m in enumerate(MEM)] + \
                       [(s_hid[par], j, "hid", m, M0 + m) for j, m in enumerate(HID)] + \
                       [(s_out[par], j, "gi", m, M0 + m) for j, m in enumerate(OUT)] + \
                       [(s_cand[par], j, "f", None, M0 + m) for j, m in enumerate(CAND)]

            def inputs(rows, matrix, values, begun):
                for sums, j, in_bank, m, b in rows:
                    o = sums[:, :, j].rearrange("p t q b -> p t (q b)")
                    ins = mm(o, ident[:, :], bias_mv[:, b].rearrange("p t q b -> p t (q b)"), in_bank not in begun)
                    begun.add(in_bank)
                    if m is None:
                        continue
                    for q in range(PART):
                        for k in range(K):
                            ins = mm(o, tile(matrix, q, k, m), values[:, :, k].rearrange("p t q b -> p t (q b)"))
                return ins

            def recurrent(sums, tiles, matrix, h):
                for j, m in enumerate(tiles):
                    for q in range(PART):
                        for k in range(K):
                            ins = mm(sums[:, j].rearrange("p q b -> p (q b)"), tile(matrix, q, k, m),
                                     h[:, k].rearrange("p q b -> p (q b)"))
                return ins

            pe.wait_ge(ident_ready, 1)
            pe.wait_ge(bias_ready, 1)
            pe.wait_ge(hi_ready, DONE["wx0"])
            pe.wait_ge(lo_ready, DONE["wx0"])
            pe.wait_ge(x_split, 1)
            inputs(first_layer(0), "wx0", x_parts[:, 0], set()).then_inc(x_used, 1)
            pe.wait_ge(hi_ready, len(SPLITS))
            pe.wait_ge(lo_ready, len(SPLITS))
            pe.wait_ge(state_ready, 2)

            def slot(base, b4, t):
                n = when(base, t)
                u = t - LAG
                c, tt = t // CH, t % CH
                g0, g1 = c % 2, (c - LAG // CH) % 2
                if n is None or n < STEPS:
                    if n != 0:
                        pe.wait_ge(h0_ready, base + t)
                    recurrent(s_gi[g0][:, tt], GI, "wh0", h0_parts).then_inc(gi_summed, 1)
                    recurrent(s_f[g0][:, tt], F, "wh0", h0_parts).then_inc(f_summed, 1)
                    recurrent(s_o[g0][:, tt], O, "wh0", h0_parts).then_inc(o_summed, 1)
                if n is None or LAG <= n < STEPS + LAG:
                    if n != LAG:
                        pe.wait_ge(h1_ready, base + u)
                    recurrent(s_hid[g1][:, tt], HID, "wh1", h1_parts).then_inc(hid_summed, 1)
                    if n is None or n < STEPS:
                        pe.wait_ge(z_f_ready, base + t + 1)
                    recurrent(s_cand[g1][:, tt], CAND, "wh1", h1_parts).then_inc(cand_summed, 1)
                    recurrent(s_out[g1][:, tt], OUT, "wh1", h1_parts).then_inc(out_summed, 1)
                more = n is None or c + 1 < STEPS // CH
                other = (c + 1) % 2
                if more and tt == 0:
                    pe.wait_ge(x_split, b4 + c + 2)
                    inputs(first_layer(other)[:4], "wx0", x_parts[:, other], set())
                if more and tt == 1:
                    inputs(first_layer(other)[4:], "wx0", x_parts[:, other], {"gi"}).then_inc(x_used, 1)
                if n is None or 1 <= c <= STEPS // CH:
                    rows = second_layer(other)
                    begun = {"gi", "f"} if more else set()
                    if tt == 2:
                        pe.wait_ge(x1_split, b4 + c)
                        inputs(rows[:2], "wx1", x1_parts[:, other], begun).then_inc(mem_summed, 1)
                        inputs(rows[2:4], "wx1", x1_parts[:, other], begun)
                    if tt == 3:
                        pe.wait_ge(xm_ready, b4 + c)
                        inputs(rows[4:], "wx1", x1_parts[:, other], begun | {"gi"}).then_inc(x1_used, 1)

            slots(pe, slot)


def kernel(x, cond_1024, L0_cond_Wx, L0_cond_Wh, L0_cond_b, L1_cond_w_W, L1_cond_w_b,
           L1_cond_wx_W, L1_cond_wx_b, L1_cond_wh_W, L1_cond_wh_b):
    import numpy as np
    import concourse.bacc as bacc
    from concourse import mybir as _mybir
    from concourse.bass_utils import run_bass_kernel_spmd

    n, steps, d = x.shape
    p, k = 128, d // 128

    def matrix(w):
        w = np.asarray(w)
        return np.ascontiguousarray(w.reshape(k, p, -1).transpose(1, 0, 2))

    def column(b):
        return np.asarray(b).reshape(-1, p).T

    w_W = np.asarray(L1_cond_w_W)
    arrays = {
        "x": np.ascontiguousarray(np.asarray(x).reshape(n, steps, k, p).transpose(3, 1, 2, 0)).reshape(p, -1),
        "state0": np.ascontiguousarray(np.asarray(cond_1024).reshape(n, k, p).transpose(2, 1, 0)).reshape(p, -1),
        "wx0": matrix(L0_cond_Wx), "wh0": matrix(L0_cond_Wh),
        "b0": np.ascontiguousarray(column(L0_cond_b)),
        "wx1": matrix(np.concatenate([w_W[:d], np.asarray(L1_cond_wx_W)], axis=1)),
        "wh1": matrix(np.concatenate([w_W[d:], np.asarray(L1_cond_wh_W)], axis=1)),
        "b1": np.ascontiguousarray(np.concatenate(
            [column(L1_cond_w_b), column(L1_cond_wh_b), column(L1_cond_wx_b)], axis=1)),
    }
    nc = bacc.Bacc("TRN2", target_bir_lowering=False, num_devices=1)
    args = [nc.dram_tensor(name, a.shape, _mybir.dt.float32, kind="ExternalInput").ap() for name, a in arrays.items()]
    out = nc.dram_tensor("out", [p, steps * k * n], _mybir.dt.float32, kind="ExternalOutput").ap()
    recurrent_layers(nc, *args, out)
    r = run_bass_kernel_spmd(nc, [arrays], core_ids=[0])
    got = np.asarray(r.results[0]["out"]).reshape(p, steps, k, n)
    return np.ascontiguousarray(got.transpose(3, 1, 2, 0)).reshape(n, steps, d)
```

```python
import concourse.bass as bass
from concourse import mybir
from contextlib import ExitStack


def recurrent_layers(nc, x, state0, wx0, wh0, wx1, wh1, biases, out):
    F32 = mybir.dt.float32
    F16 = mybir.dt.float16
    ALU = mybir.AluOpType
    ACT = mybir.ActivationFunctionType
    AX = mybir.AxisListType

    P = 128
    STEPS = 512
    B = 8
    K = 2
    S = K * B
    PART = 2
    CH = 4
    CHUNK = CH * S
    LAG = 2 * CH
    RING = 2 * CH
    BODY = 4 * CH
    M0, M1 = 8, 6
    G, I, F, O = [6, 7], [0, 1], [2, 3], [4, 5]
    HID, OUT, CAND, MEM = [0, 1], [2, 3], [4, 5], [4, 5]

    VS = 64.0
    WS = 64.0
    ACC = VS * WS

    ctx = ExitStack()
    with ctx:
        def sb(name, shape, dt=F32):
            return ctx.enter_context(nc.sbuf_tensor(name, shape, dt))

        def sem(name):
            return ctx.enter_context(nc.semaphore(name))

        xs = sb("xs", [P, STEPS * S])
        stage = sb("stage", [P, 2 * K * (M0 + M1) * P])
        WCOLS = {"wx0": M0 * P, "wh0": M0 * P, "wx1": M1 * P, "wh1": M1 * P}
        wparts = {n: sb(n + "_parts", [P, PART, K, c], F16) for n, c in WCOLS.items()}
        NB, LOW = M0 + M1 + K, 32
        bias = sb("bias", [2 * LOW, P])
        bias_rows = sb("bias_rows", [2 * LOW, P], F16)
        full = sb("full", [2 * LOW, NB, CH, B], F16)
        chosen = sb("chosen", [2 * LOW, NB, CH, B], F16)
        cond = sb("cond", [P, S])
        x_parts = sb("x_parts", [P, 2, CH, K, PART, B], F16)
        x1_parts = sb("x1_parts", [P, 2, CH, K, PART, B], F16)
        h0_parts = sb("h0_parts", [P, K, PART, B], F16)
        h1_parts = sb("h1_parts", [P, K, PART, B], F16)
        h0_all = sb("h0_all", [P, RING, S])
        h1_all = sb("h1_all", [P, RING, S, 2])
        z_g = sb("z_g", [P, S])
        z_i = sb("z_i", [P, S])
        z_f = sb("z_f", [P, S])
        z_o = sb("z_o", [P, S])
        g_new = sb("g_new", [P, S])
        i_gate = sb("i_gate", [P, S])
        o_gate = sb("o_gate", [P, S])
        cell_pairs = [sb(f"cell_pairs{i}", [P, 2 * S + 2]) for i in range(2)]
        f_pairs = sb("f_pairs", [P, 2 * S])
        t_cell = sb("t_cell", [P, S])
        z_hid = sb("z_hid", [P, S])
        z_out = sb("z_out", [P, S])
        mem_pairs = sb("mem_pairs", [P, 2, CH, S, 2])
        hid_pairs = sb("hid_pairs", [P, 2 * S])
        mem = sb("mem", [P, 2 * S])
        out_pairs = sb("out_pairs", [P, 2 * S])
        mix_pairs = sb("mix_pairs", [P, 2 * S])

        def bank(name):
            return ctx.enter_context(nc.psum_tensor(name, [P, 512], F32))

        WIDTH = CH * PART * B
        b_i = [bank(f"b_i_mem{i}") for i in range(2)]
        b_f = [bank(f"b_f_cand{i}") for i in range(2)]
        b_g = [bank(f"b_g_hid{i}") for i in range(2)]
        b_o = [bank(f"b_o_out{i}") for i in range(2)]
        BANKS = [b_i, b_f, b_g, b_o]

        def cols(banks, first, tiles):
            return [t[:, first * WIDTH:(first + tiles) * WIDTH]
                    .rearrange("p (t m q b) -> p t m q b", t=CH, m=tiles, q=PART) for t in banks]

        s_i, s_mem = cols(b_i, 0, K), cols(b_i, K, K)
        s_f, s_cand = cols(b_f, 0, K), cols(b_f, K, K)
        s_g, s_hid = cols(b_g, 0, K), cols(b_g, K, K)
        s_o, s_out = cols(b_o, 0, K), cols(b_o, K, K)

        dma_x0, dma_x, dma_small = sem("dma_x0"), sem("dma_x"), sem("dma_small")
        dma_w = {n: sem("dma_" + n) for n in WCOLS}
        out_stored = sem("out_stored")
        rows_zero, full_set, chosen_ready = sem("rows_zero"), sem("full_set"), sem("chosen_ready")
        hi_ready, lo_ready = sem("hi_ready"), sem("lo_ready")
        factors_zero = sem("factors_zero")
        bias_split, bias_ready = sem("bias_split"), sem("bias_ready")
        state_hi, state_ready = sem("state_hi"), sem("state_ready")
        h0_ready, h0_whole = sem("h0_ready"), sem("h0_whole")
        g_summed, i_summed, f_summed, o_summed = sem("g_summed"), sem("i_summed"), sem("f_summed"), sem("o_summed")
        z_g_ready, z_i_ready, z_f_ready, z_o_ready = sem("z_g_ready"), sem("z_i_ready"), sem("z_f_ready"), sem("z_o_ready")
        gi_ready, cell_tanh = sem("gi_ready"), sem("cell_tanh")
        cell_terms, cell_ready = sem("cell_terms"), sem("cell_ready")
        h1_ready, h1_whole, h1_high = sem("h1_ready"), sem("h1_whole"), sem("h1_high")
        hid_summed, cand_summed, out_summed = sem("hid_summed"), sem("cand_summed"), sem("out_summed")
        z_hid_ready, z_out_ready = sem("z_hid_ready"), sem("z_out_ready")
        mem_terms = sem("mem_terms")
        mem_tanh = sem("mem_tanh")
        mix_terms = sem("mix_terms")
        mem_ready = sem("mem_ready")
        x_hi, x_split = sem("x_hi"), sem("x_split")
        x1_hi, x1_split = sem("x1_hi"), sem("x1_split")
        mem_summed, out_ready = sem("mem_summed"), sem("out_ready")

        STAGE_AT, at = {}, 0
        for n, c in WCOLS.items():
            STAGE_AT[n] = at
            at += K * c

        def staged(n):
            return stage[:, STAGE_AT[n]:STAGE_AT[n] + K * WCOLS[n]].rearrange("p (k c) -> p k c", k=K)

        SPLITS = [("wx0", 0, 4 * K * P), ("wh0", 0, 4 * K * P), ("wx1", 0, 3 * K * P), ("wh1", 0, 3 * K * P)]
        DONE = {n: 1 + max(i for i, s in enumerate(SPLITS) if s[0] == n) for n in WCOLS}

        FIRST = 4 * CH
        REST = FIRST - 2 * CH
        block = ctx.enter_context(nc.Block())

        LOOP_FROM, LOOP_TO = BODY, STEPS - BODY

        def slots(eng, slot, twice=False):
            for t in range(LOOP_FROM):
                slot(0, 0, t)
            with eng.Fori(LOOP_FROM // BODY, LOOP_TO // BODY, 1) as turn:
                base, base_c = eng.snap(turn * BODY), eng.snap(turn * (BODY // CH))
                more = [eng.snap(turn * (2 * BODY))] if twice else []
                for t in range(BODY):
                    slot(base, base_c, t, *more)
            for t in range(LOOP_TO, STEPS + LAG + 1):
                slot(0, 0, t)

        def when(base, t):
            return None if not isinstance(base, int) else t

        def chunk_of(c0, c):
            return xs[:, bass.ds(c0 * CHUNK + c * CHUNK, CHUNK)]

        def pair(t, par, q):
            return t[:, par].rearrange("p t k q b -> p q (t k) b")[:, q]

        def odd(t):
            return t[:, :].rearrange("p (s two) -> p s two", two=2)[:, :, 1]

        def even(t):
            return t[:, :].rearrange("p (s two) -> p s two", two=2)[:, :, 0]

        def cell_of(t):
            return cell_pairs[t % 2][:, 1:1 + 2 * S].rearrange("p (s two) -> p s two", two=2)[:, :, 0]

        @block.sync
        def _(sp):
            def rows(a, lo, hi):
                return a[:, lo:hi]

            sp.dma_start(staged("wx0"), wx0).then_inc(dma_w["wx0"], 16)
            sp.dma_start(xs[:, 0:FIRST * S], rows(x, 0, FIRST * S)).then_inc(dma_x0, 16)
            sp.dma_start(cond[:, :], state0).then_inc(dma_small, 16)
            for at in (0, LOW):
                sp.dma_start(bias[at:at + NB, :], biases).then_inc(dma_small, 16)
            sp.dma_start(staged("wh0"), wh0).then_inc(dma_w["wh0"], 16)
            sp.dma_start(staged("wx1"), wx1).then_inc(dma_w["wx1"], 16)
            sp.dma_start(staged("wh1"), wh1).then_inc(dma_w["wh1"], 16)
            sp.dma_start(xs[:, FIRST * S:], rows(x, FIRST * S, STEPS * S)).then_inc(dma_x, 16)
            W, CHUNKS = BODY * S, BODY // CH
            with sp.Fori(0, STEPS // BODY, 1) as n:
                sp.wait_ge(out_ready, n * CHUNKS + CHUNKS)
                sp.dma_start(out[:, bass.ds(n * W, W)], xs[:, bass.ds(n * W, W)]).then_inc(out_stored, 16)
            sp.wait_ge(out_stored, 16 * (STEPS // BODY))

        @block.gpsimd
        def _(pool):
            pool.memset(bias_rows[:, :], 0.0).then_inc(rows_zero, 1)
            pool.memset(f_pairs[:, :], 0.0)
            pool.memset(out_pairs[:, :], 0.0)
            pool.memset(hid_pairs[:, :], 0.0).then_inc(factors_zero, 1)
            pool.memset(full[:, :, :, :], VS).then_inc(full_set, 1)
            pool.wait_ge(full_set, 1)
            for at in (0, LOW):
                pool.affine_select(out=chosen[at:at + LOW], in_=full[at:at + LOW], compare_op=ALU.is_equal, fill=0.0,
                                   base=0, pattern=[[-1, NB], [0, CH], [0, B]], channel_multiplier=1).then_inc(chosen_ready, 1)

        @block.scalar
        def _(act):
            def x_high(c, b4):
                act.activation(pair(x_parts, c % 2, 0), chunk_of(b4, c).rearrange("p (a b) -> p a b", b=B),
                               ACT.Copy, scale=VS).then_inc(x_hi, 1)

            act.wait_ge(dma_x0, 16)
            for c in range(2):
                x_high(c, 0)
            for n, lo, hi in SPLITS:
                act.wait_ge(dma_w[n], 16)
                act.activation(wparts[n][:, 0, :, lo:hi], staged(n)[:, :, lo:hi], ACT.Copy, scale=WS).then_inc(hi_ready, 1)

            act.wait_ge(factors_zero, 1)

            def tanh(out_, in_, scale=1 / ACC):
                return act.activation(out_, in_, ACT.Tanh, scale=scale)

            def sigmoid(out_, in_):
                return act.activation(out_, in_, ACT.Sigmoid, scale=1 / ACC)

            def slot(base, b4, t):
                n = when(base, t)
                u = t - LAG
                c, tt = t // CH, t % CH
                l0 = n is None or n < STEPS
                l1 = n is None or LAG <= n < STEPS + LAG
                if l0:
                    act.wait_ge(z_g_ready, base + t + 1)
                    tanh(g_new[:, :], z_g[:, :])
                    act.wait_ge(z_i_ready, base + t + 1)
                    sigmoid(i_gate[:, :], z_i[:, :]).then_inc(gi_ready, 1)
                    act.wait_ge(z_f_ready, base + t + 1)
                    sigmoid(odd(f_pairs), z_f[:, :]).then_inc(cell_terms, 1)
                    act.wait_ge(z_o_ready, base + t + 1)
                    sigmoid(o_gate[:, :], z_o[:, :])
                    act.wait_ge(cell_ready, base + t + 1)
                    tanh(t_cell[:, :], cell_of(t + 1), 1.0).then_inc(cell_tanh, 1)
                if l1:
                    act.wait_ge(z_hid_ready, base + u + 1)
                    sigmoid(odd(hid_pairs), z_hid[:, :]).then_inc(mem_terms, 1)
                if l1:
                    act.wait_ge(mem_ready, base + u + 1)
                    tanh(odd(mix_pairs), odd(mem)).then_inc(mem_tanh, 1)
                    act.wait_ge(z_out_ready, base + u + 1)
                    sigmoid(odd(out_pairs), z_out[:, :]).then_inc(mix_terms, 1)
                if n == REST:
                    act.wait_ge(dma_x, 16)
                if tt == 1 and (n is None or c + 2 < STEPS // CH):
                    x_high(c + 2, b4)
                if tt == 0 and (n is None or 1 <= c <= STEPS // CH):
                    act.activation(pair(x1_parts, (c - 1) % 2, 0), chunk_of(b4, c - 1).rearrange("p (a b) -> p a b", b=B),
                                   ACT.Copy, scale=VS).then_inc(x1_hi, 1)

            slots(act, slot)

        @block.vector
        def _(dve):
            V = nc.vector

            def parts(t, q):
                return t.rearrange("p k q b -> p q k b")[:, q]

            def add_parts(z, sums, done):
                V.tensor_reduce(z.rearrange("p (m b) -> p m b", b=B), sums.rearrange("p m q b -> p m b q"),
                                AX.X, ALU.add).then_inc(done, 1)

            def heads(t):
                return t.rearrange("p (k b) -> p k b", k=K)

            def pairs_of(t):
                return cell_pairs[t % 2][:, 1:1 + 2 * S].rearrange("p (s two) -> p s two", two=2)

            def steps_of(t, c):
                first = (c % 2) * CH
                return t[:, first:first + CH, :].rearrange("p t s -> p (t s)")

            def low(i):
                n, lo, hi = SPLITS[i]
                dve.wait_ge(hi_ready, i + 1)
                for k in range(K):
                    ins = V.scalar_tensor_tensor(out=wparts[n][:, 1, k, lo:hi], in0=staged(n)[:, k, lo:hi], scalar=WS,
                                                 in1=wparts[n][:, 0, k, lo:hi], op0=ALU.mult, op1=ALU.subtract)
                ins.then_inc(lo_ready, 1)

            def x_low(c, b4):
                dve.wait_ge(x_hi, b4 + c + 1)
                V.scalar_tensor_tensor(out=pair(x_parts, c % 2, 1),
                                       in0=chunk_of(b4, c).rearrange("p (a b) -> p a b", b=B), scalar=VS,
                                       in1=pair(x_parts, c % 2, 0), op0=ALU.mult, op1=ALU.subtract).then_inc(x_split, 1)

            dve.wait_ge(dma_x0, 16)
            for c in range(2):
                x_low(c, 0)
            low(0)

            dve.wait_ge(dma_small, 48)
            for pairs in cell_pairs:
                V.memset(pairs[:, :], 0.0)
            c3 = heads(cond[:, :])
            V.tensor_scalar_mul(parts(h0_parts, 0), c3, VS)
            V.tensor_scalar_mul(parts(h1_parts, 0), c3, VS)
            V.tensor_copy(h1_all[:, (LAG - 1) % RING, :, 1], cond[:, :]).then_inc(state_hi, 1)
            dve.wait_ge(rows_zero, 1)
            V.tensor_scalar_mul(bias_rows[0:NB, :], bias[0:NB, :], WS)
            V.tensor_scalar_mul(bias_rows[LOW:LOW + NB, :], bias[LOW:LOW + NB, :], WS).then_inc(bias_split, 1)
            dve.wait_ge(state_hi, 1)
            for h in (h0_parts, h1_parts):
                V.scalar_tensor_tensor(out=parts(h, 1), in0=c3, scalar=VS, in1=parts(h, 0),
                                       op0=ALU.mult, op1=ALU.subtract).then_inc(state_ready, 1)
            dve.wait_ge(bias_split, 1)
            V.scalar_tensor_tensor(out=bias_rows[LOW:LOW + NB, :], in0=bias[LOW:LOW + NB, :], scalar=WS,
                                   in1=bias_rows[LOW:LOW + NB, :], op0=ALU.mult, op1=ALU.subtract).then_inc(bias_ready, 1)

            for i in range(1, len(SPLITS)):
                low(i)

            def slot(base, b4, t, base2=0):
                n = when(base, t)
                u = t - LAG
                i0, i1 = t % RING, (t - 1) % RING
                c, tt = t // CH, t % CH
                l0 = n is None or n < STEPS
                l1 = n is None or LAG <= n < STEPS + LAG
                l1_before = n is None or LAG < n <= STEPS + LAG
                more_x = n is None or c + 2 < STEPS // CH
                have_x1 = n is None or 1 <= c <= STEPS // CH
                g0, g1 = c % 2, (c - LAG // CH) % 2

                if n == REST:
                    dve.wait_ge(dma_x, 16)
                if l1_before:
                    dve.wait_ge(mix_terms, base2 + 2 * u)
                    V.tensor_tensor_scan(out=h1_all[:, i1].rearrange("p s two -> p (s two)"), data0=out_pairs[:, :],
                                         data1=mix_pairs[:, :], initial=0.0, op0=ALU.mult, op1=ALU.add).then_inc(h1_whole, 1)
                if l0:
                    dve.wait_ge(g_summed, base + t + 1)
                    add_parts(z_g[:, :], s_g[g0][:, tt], z_g_ready)
                if l1_before:
                    dve.wait_ge(h1_whole, base + u)
                    V.tensor_scalar_mul(parts(h1_parts, 0), heads(h1_all[:, i1, :, 1]), VS).then_inc(h1_high, 1)
                if l0:
                    dve.wait_ge(i_summed, base + t + 1)
                    add_parts(z_i[:, :], s_i[g0][:, tt], z_i_ready)
                if l1_before:
                    dve.wait_ge(h1_high, base + u)
                    V.scalar_tensor_tensor(out=parts(h1_parts, 1), in0=heads(h1_all[:, i1, :, 1]), scalar=VS,
                                           in1=parts(h1_parts, 0), op0=ALU.mult, op1=ALU.subtract).then_inc(h1_ready, 1)
                if l0:
                    dve.wait_ge(f_summed, base + t + 1)
                    add_parts(z_f[:, :], s_f[g0][:, tt], z_f_ready)

                here = chunk_of(b4, c - 1) if have_x1 else None
                if tt == 0 and have_x1:
                    V.tensor_tensor(here, steps_of(h0_all, c - 1), here, ALU.add)
                if tt == 1 and have_x1:
                    dve.wait_ge(x1_hi, b4 + c)
                    V.scalar_tensor_tensor(out=pair(x1_parts, (c - 1) % 2, 1), in0=here.rearrange("p (a b) -> p a b", b=B),
                                           scalar=VS, in1=pair(x1_parts, (c - 1) % 2, 0), op0=ALU.mult,
                                           op1=ALU.subtract).then_inc(x1_split, 1)
                if tt == 2 and more_x:
                    x_low(c + 2, b4)
                if tt == 3 and have_x1:
                    dve.wait_ge(mem_summed, b4 + c)
                    V.tensor_reduce(mem_pairs[:, (c - 1) % 2, :, :, 1].rearrange("p t (m b) -> p (t m) b", b=B),
                                    s_mem[(c - 1) % 2].rearrange("p t m q b -> p (t m) b q"), AX.X, ALU.add)

                if l0:
                    dve.wait_ge(gi_ready, base + t + 1)
                    V.tensor_tensor(pairs_of(t)[:, :, 1], i_gate[:, :], g_new[:, :], ALU.mult).then_inc(cell_terms, 1)
                    dve.wait_ge(o_summed, base + t + 1)
                    add_parts(z_o[:, :], s_o[g0][:, tt], z_o_ready)
                    dve.wait_ge(cell_terms, base2 + 2 * t + 2)
                    V.tensor_tensor_scan(out=cell_pairs[(t + 1) % 2][:, 0:2 * S], data0=f_pairs[:, :],
                                         data1=cell_pairs[t % 2][:, 1:1 + 2 * S], initial=0.0,
                                         op0=ALU.mult, op1=ALU.add).then_inc(cell_ready, 1)
                if l1:
                    dve.wait_ge(hid_summed, base + u + 1)
                    add_parts(z_hid[:, :], s_hid[g1][:, tt], z_hid_ready)
                    dve.wait_ge(cand_summed, base + u + 1)
                    V.tensor_reduce(mem_pairs[:, g1, tt, :, 0].rearrange("p (m b) -> p m b", b=B),
                                    s_cand[g1][:, tt].rearrange("p m q b -> p m b q"), AX.X, ALU.add).then_inc(mem_terms, 1)
                if l0:
                    dve.wait_ge(cell_tanh, base + t + 1)
                    V.scalar_tensor_tensor(out=parts(h0_parts, 0), in0=heads(o_gate[:, :]), scalar=VS,
                                           in1=heads(t_cell[:, :]), op0=ALU.mult, op1=ALU.mult)
                    V.tensor_tensor(h0_all[:, i0, :], o_gate[:, :], t_cell[:, :], ALU.mult).then_inc(h0_whole, 1)
                if l1:
                    dve.wait_ge(mem_terms, base2 + 2 * u + 2)
                    V.tensor_tensor_scan(out=mem[:, :], data0=hid_pairs[:, :],
                                         data1=mem_pairs[:, g1, tt].rearrange("p s two -> p (s two)"), initial=0.0,
                                         op0=ALU.mult, op1=ALU.add).then_inc(mem_ready, 1)
                if l0:
                    dve.wait_ge(h0_whole, base + t + 1)
                    V.scalar_tensor_tensor(out=parts(h0_parts, 1), in0=heads(h0_all[:, i0, :]), scalar=VS,
                                           in1=parts(h0_parts, 0), op0=ALU.mult, op1=ALU.subtract).then_inc(h0_ready, 1)
                if l1:
                    dve.wait_ge(out_summed, base + u + 1)
                    add_parts(z_out[:, :], s_out[g1][:, tt], z_out_ready)
                    dve.wait_ge(mem_tanh, base + u + 1)
                    V.tensor_tensor(even(mix_pairs), h1_all[:, i1, :, 1], odd(mix_pairs), ALU.subtract).then_inc(mix_terms, 1)

                if (tt == 2 and (n is None or 3 <= c)) or (n is not None and n == STEPS + LAG):
                    result = chunk_of(b4, c - 3)
                    first = (c - 3) % 2 * CH
                    V.tensor_tensor(result, h1_all[:, first:first + CH, :, 1].rearrange("p t s -> p (t s)"), result,
                                    ALU.add).then_inc(out_ready, 1)

            slots(dve, slot, twice=True)

        @block.tensor
        def _(pe):
            def mm(o, w, rhs, start=False):
                return nc.tensor.matmul(o, w, rhs, start=start, stop=True, skip_group_check=True)

            def tile(n, q, k, m):
                return wparts[n][:, q, k, m * P:(m + 1) * P]

            def biases_in(par, lo, hi):
                for i in range(lo, hi):
                    for j in range(2):
                        o = BANKS[i][par][:, j * K * WIDTH:(j + 1) * K * WIDTH] \
                            .rearrange("p (t m q b) -> p m t q b", t=CH, m=K, q=PART)[:, :, :, 0]
                        mm(o, bias_rows[:, :], chosen[:, (2 * i + j) * K:(2 * i + j + 1) * K], j == 0)

            def first_layer(par):
                return [(s[par], j, m) for s, ms in ((s_g, G), (s_i, I), (s_f, F), (s_o, O)) for j, m in enumerate(ms)]

            def second_layer(par):
                return [(s[par], j, m) for s, ms in ((s_mem, MEM), (s_hid, HID), (s_out, OUT)) for j, m in enumerate(ms)]

            PER = PART * K

            def inputs(rows, matrix, values, lo, hi):
                for n in range(lo, hi):
                    sums, j, m = rows[n // PER]
                    q, k = n % PER // K, n % K
                    ins = mm(sums[:, :, j].rearrange("p t q b -> p t (q b)"), tile(matrix, q, k, m),
                             values[:, :, k].rearrange("p t q b -> p t (q b)"))
                return ins

            def recurrent(sums, tiles, matrix, h):
                for j, m in enumerate(tiles):
                    for q in range(PART):
                        for k in range(K):
                            ins = mm(sums[:, j].rearrange("p q b -> p (q b)"), tile(matrix, q, k, m),
                                     h[:, k].rearrange("p q b -> p (q b)"))
                return ins

            pe.wait_ge(chosen_ready, 2)
            pe.wait_ge(bias_ready, 1)
            biases_in(0, 0, len(BANKS))
            pe.wait_ge(hi_ready, DONE["wx0"])
            pe.wait_ge(lo_ready, DONE["wx0"])
            pe.wait_ge(x_split, 1)
            inputs(first_layer(0), "wx0", x_parts[:, 0], 0, M0 * PER)
            pe.wait_ge(hi_ready, len(SPLITS))
            pe.wait_ge(lo_ready, len(SPLITS))
            pe.wait_ge(state_ready, 2)

            def slot(base, b4, t):
                n = when(base, t)
                u = t - LAG
                c, tt = t // CH, t % CH
                g0, g1 = c % 2, (c - LAG // CH) % 2
                other = (c + 1) % 2
                more = n is None or c + 1 < STEPS // CH
                have_x1 = n is None or 1 <= c <= STEPS // CH
                def x_products(lo, hi):
                    return inputs(first_layer(other), "wx0", x_parts[:, other], lo, hi)

                def x1_products(lo, hi):
                    return inputs(second_layer(other), "wx1", x1_parts[:, other], lo, hi)

                if n is None or n < STEPS:
                    if n != 0:
                        pe.wait_ge(h0_ready, base + t)
                    recurrent(s_g[g0][:, tt], G, "wh0", h0_parts).then_inc(g_summed, 1)
                    recurrent(s_i[g0][:, tt], I, "wh0", h0_parts).then_inc(i_summed, 1)
                    recurrent(s_f[g0][:, tt], F, "wh0", h0_parts).then_inc(f_summed, 1)
                    if n is None or n > LAG:
                        pe.wait_ge(z_out_ready, base + u)
                    recurrent(s_o[g0][:, tt], O, "wh0", h0_parts).then_inc(o_summed, 1)

                if tt == 0 and more:
                    biases_in(other, 0, 1)
                if tt == 1 and more:
                    x_products(9, 12)
                if tt == 2 and more:
                    x_products(24, 27)
                if tt == 3 and have_x1:
                    x1_products(10, 13)

                if n is None or LAG <= n < STEPS + LAG:
                    if n != LAG:
                        pe.wait_ge(h1_ready, base + u)
                    else:
                        pe.wait_ge(z_g_ready, base + t + 1)
                    recurrent(s_hid[g1][:, tt], HID, "wh1", h1_parts).then_inc(hid_summed, 1)
                    if n is None or n < STEPS:
                        pe.wait_ge(z_f_ready, base + t + 1)
                    recurrent(s_cand[g1][:, tt], CAND, "wh1", h1_parts).then_inc(cand_summed, 1)
                    if n is None or n < STEPS:
                        pe.wait_ge(z_o_ready, base + t + 1)
                    recurrent(s_out[g1][:, tt], OUT, "wh1", h1_parts).then_inc(out_summed, 1)

                if tt == 0 and (more or have_x1):
                    biases_in(other, 1 if more else 0, len(BANKS))
                if tt == 0 and more:
                    pe.wait_ge(x_split, b4 + c + 2)
                    x_products(0, 9)
                if tt == 1 and more:
                    x_products(12, 24)
                if tt == 2 and more:
                    x_products(27, M0 * PER)
                if tt == 2 and have_x1:
                    pe.wait_ge(x1_split, b4 + c)
                    x1_products(0, 2 * PER).then_inc(mem_summed, 1)
                    x1_products(2 * PER, 10)
                if tt == 3 and have_x1:
                    x1_products(13, M1 * PER)

            slots(pe, slot)


def kernel(x, cond_1024, L0_cond_Wx, L0_cond_Wh, L0_cond_b, L1_cond_w_W, L1_cond_w_b,
           L1_cond_wx_W, L1_cond_wx_b, L1_cond_wh_W, L1_cond_wh_b):
    import numpy as np
    import concourse.bacc as bacc
    from concourse import mybir as _mybir
    from concourse.bass_utils import run_bass_kernel_spmd

    n, steps, d = x.shape
    p, k = 128, d // 128

    def matrix(w):
        w = np.asarray(w)
        return np.ascontiguousarray(w.reshape(k, p, -1).transpose(1, 0, 2))

    b0, b_w = np.asarray(L0_cond_b), np.asarray(L1_cond_w_b)
    w_W = np.asarray(L1_cond_w_W)
    arrays = {
        "x": np.ascontiguousarray(np.asarray(x).reshape(n, steps, k, p).transpose(3, 1, 2, 0)).reshape(p, -1),
        "state0": np.ascontiguousarray(np.asarray(cond_1024).reshape(n, k, p).transpose(2, 1, 0)).reshape(p, -1),
        "wx0": matrix(L0_cond_Wx), "wh0": matrix(L0_cond_Wh),
        "wx1": matrix(np.concatenate([w_W[:d], np.asarray(L1_cond_wx_W)], axis=1)),
        "wh1": matrix(np.concatenate([w_W[d:], np.asarray(L1_cond_wh_W)], axis=1)),
        "biases": np.concatenate([np.asarray(v).reshape(-1, p) for v in (
            b0[0:d], L1_cond_wx_b, b0[d:2 * d], L1_cond_wh_b, b0[3 * d:], b_w[:d], b0[2 * d:3 * d], b_w[d:])]),
    }
    nc = bacc.Bacc("TRN2", target_bir_lowering=False, num_devices=1)
    args = [nc.dram_tensor(name, a.shape, _mybir.dt.float32, kind="ExternalInput").ap() for name, a in arrays.items()]
    out = nc.dram_tensor("out", [p, steps * k * n], _mybir.dt.float32, kind="ExternalOutput").ap()
    recurrent_layers(nc, *args, out)
    r = run_bass_kernel_spmd(nc, [arrays], core_ids=[0])
    got = np.asarray(r.results[0]["out"]).reshape(p, steps, k, n)
    return np.ascontiguousarray(got.transpose(3, 1, 2, 0)).reshape(n, steps, d)
```
